# Optimizing a Trainium2 kernel written in Bass

```python
import numpy as np
import jax
import jax.numpy as jnp

def _softmax(x, axis=-1):
    return jax.nn.softmax(x, axis=axis)

def _gelu(x):
    return jax.nn.gelu(x, approximate=True)

def _silu(x):
    return jax.nn.silu(x)

def _sigmoid(x):
    return jax.nn.sigmoid(x)

def _layernorm(x, axis=-1, eps=1e-05):
    m = jnp.mean(x, axis=axis, keepdims=True)
    v = jnp.var(x, axis=axis, keepdims=True)
    return (x - m) / jnp.sqrt(v + eps)

def _scatter_add(tgt, idx, src, axis=0):
    return tgt.at[idx].add(src)

def _segment_sum(src, seg, n):
    return jax.ops.segment_sum(src, seg, n)
kernel_name = 'mk_rec_standalone_d1_rec_r8_22fc6d'

def setup_inputs(seed: int=0):
    np.random.seed(seed)
    _w = jnp.asarray

    def _rec_inputs():
        import jax
        import jax.numpy as jnp
        _rk = jax.random.key(seed)
        r_dense = -0.00493535 + 1.00056 * jax.random.normal(jax.random.fold_in(_rk, 1), (2048, 16), jnp.float32)
        r_sparse = jnp.stack([jax.random.randint(jax.random.fold_in(jax.random.fold_in(_rk, 2), 0), (2048,), 9, 49979, jnp.int32), jax.random.randint(jax.random.fold_in(jax.random.fold_in(_rk, 2), 1), (2048,), 16, 49996, jnp.int32), jax.random.randint(jax.random.fold_in(jax.random.fold_in(_rk, 2), 2), (2048,), 13, 49978, jnp.int32), jax.random.randint(jax.random.fold_in(jax.random.fold_in(_rk, 2), 3), (2048,), 2, 49991, jnp.int32), jax.random.randint(jax.random.fold_in(jax.random.fold_in(_rk, 2), 4), (2048,), 0, 49990, jnp.int32), jax.random.randint(jax.random.fold_in(jax.random.fold_in(_rk, 2), 5), (2048,), 15, 49999, jnp.int32), jax.random.randint(jax.random.fold_in(jax.random.fold_in(_rk, 2), 6), (2048,), 19, 6250, jnp.int32), jax.random.randint(jax.random.fold_in(jax.random.fold_in(_rk, 2), 7), (2048,), 1, 49993, jnp.int32), jax.random.randint(jax.random.fold_in(jax.random.fold_in(_rk, 2), 8), (2048,), 28, 49950, jnp.int32), jax.random.randint(jax.random.fold_in(jax.random.fold_in(_rk, 2), 9), (2048,), 0, 49993, jnp.int32), jax.random.randint(jax.random.fold_in(jax.random.fold_in(_rk, 2), 10), (2048,), 6, 49998, jnp.int32), jax.random.randint(jax.random.fold_in(jax.random.fold_in(_rk, 2), 11), (2048,), 4, 49963, jnp.int32), jax.random.randint(jax.random.fold_in(jax.random.fold_in(_rk, 2), 12), (2048,), 3, 49988, jnp.int32), jax.random.randint(jax.random.fold_in(jax.random.fold_in(_rk, 2), 13), (2048,), 7, 49996, jnp.int32), jax.random.randint(jax.random.fold_in(jax.random.fold_in(_rk, 2), 14), (2048,), 24, 49995, jnp.int32), jax.random.randint(jax.random.fold_in(jax.random.fold_in(_rk, 2), 15), (2048,), 1, 49995, jnp.int32), jax.random.randint(jax.random.fold_in(jax.random.fold_in(_rk, 2), 16), (2048,), 12, 49997, jnp.int32), jax.random.randint(jax.random.fold_in(jax.random.fold_in(_rk, 2), 17), (2048,), 19, 49995, jnp.int32), jax.random.randint(jax.random.fold_in(jax.random.fold_in(_rk, 2), 18), (2048,), 19, 49997, jnp.int32), jax.random.randint(jax.random.fold_in(jax.random.fold_in(_rk, 2), 19), (2048,), 5, 49991, jnp.int32), jax.random.randint(jax.random.fold_in(jax.random.fold_in(_rk, 2), 20), (2048,), 11, 49980, jnp.int32), jax.random.randint(jax.random.fold_in(jax.random.fold_in(_rk, 2), 21), (2048,), 8, 49967, jnp.int32), jax.random.randint(jax.random.fold_in(jax.random.fold_in(_rk, 2), 22), (2048,), 33, 49982, jnp.int32), jax.random.randint(jax.random.fold_in(jax.random.fold_in(_rk, 2), 23), (2048,), 2, 49982, jnp.int32), jax.random.randint(jax.random.fold_in(jax.random.fold_in(_rk, 2), 24), (2048,), 17, 49997, jnp.int32), jax.random.randint(jax.random.fold_in(jax.random.fold_in(_rk, 2), 25), (2048,), 5, 49986, jnp.int32), jax.random.randint(jax.random.fold_in(jax.random.fold_in(_rk, 2), 26), (2048,), 41, 6250, jnp.int32), jax.random.randint(jax.random.fold_in(jax.random.fold_in(_rk, 2), 27), (2048,), 3, 6250, jnp.int32), jax.random.randint(jax.random.fold_in(jax.random.fold_in(_rk, 2), 28), (2048,), 12, 49995, jnp.int32), jax.random.randint(jax.random.fold_in(jax.random.fold_in(_rk, 2), 29), (2048,), 8, 49989, jnp.int32), jax.random.randint(jax.random.fold_in(jax.random.fold_in(_rk, 2), 30), (2048,), 8, 49990, jnp.int32), jax.random.randint(jax.random.fold_in(jax.random.fold_in(_rk, 2), 31), (2048,), 0, 6250, jnp.int32)], axis=1)
        return (r_dense, r_sparse)
    r_dense, r_sparse = _rec_inputs()

    def _L0_rec_setup():
        import jax, jax.numpy as jnp
        import numpy as np
        B, F, V, E, D1, DD, L2 = (512, 32, 6250, 64, 256, 16, 128)
        key = jax.random.key(seed)
        ks = jax.random.split(key, 16)
        s = 0.05
        return {'sparse': jax.random.randint(ks[0], (B, F), 0, V, dtype=jnp.int32), 'dense': jax.random.normal(ks[1], (B, DD), dtype=jnp.float32), 'tables': jax.random.normal(ks[2], (F, V, E), dtype=jnp.float32) * s, 'Wz': jax.random.normal(ks[3], (D1, F, E), dtype=jnp.float32) * s, 'bz': jnp.zeros((D1,), jnp.float32), 'Wpi': jax.random.normal(ks[4], (D1, F, F), dtype=jnp.float32) * s, 'bpi': jnp.zeros((D1,), jnp.float32), 'Wpo': jax.random.normal(ks[5], (D1, E, E), dtype=jnp.float32) * s, 'bpo': jnp.zeros((D1,), jnp.float32), 'B1': jax.random.normal(ks[6], (D1,), dtype=jnp.float32) * s, 'W1': jax.random.normal(ks[7], (D1 + DD, D1), dtype=jnp.float32) * s, 'b1': jnp.zeros((D1,), jnp.float32), 'W2': jax.random.normal(ks[8], (D1, L2), dtype=jnp.float32) * s, 'b2': jnp.zeros((L2,), jnp.float32), 'W3': jax.random.normal(ks[9], (L2, 1), dtype=jnp.float32) * s, 'b3': jnp.zeros((1,), jnp.float32)}
    _L0_rec_all = _L0_rec_setup()
    _L0_rec_in = {k: v for k, v in _L0_rec_all.items() if k in ('tables', 'Wz', 'bz', 'Wpi', 'bpi', 'Wpo', 'bpo', 'B1', 'W1', 'b1', 'W2', 'b2', 'W3', 'b3')}
    del _L0_rec_all
    return {'r_dense': r_dense, 'r_sparse': r_sparse, 'L0_rec_tables': _L0_rec_in['tables'], 'L0_rec_Wz': _L0_rec_in['Wz'], 'L0_rec_bz': _L0_rec_in['bz'], 'L0_rec_Wpi': _L0_rec_in['Wpi'], 'L0_rec_bpi': _L0_rec_in['bpi'], 'L0_rec_Wpo': _L0_rec_in['Wpo'], 'L0_rec_bpo': _L0_rec_in['bpo'], 'L0_rec_B1': _L0_rec_in['B1'], 'L0_rec_W1': _L0_rec_in['W1'], 'L0_rec_b1': _L0_rec_in['b1'], 'L0_rec_W2': _L0_rec_in['W2'], 'L0_rec_b2': _L0_rec_in['b2'], 'L0_rec_W3': _L0_rec_in['W3'], 'L0_rec_b3': _L0_rec_in['b3']}

def reference(r_dense, r_sparse, L0_rec_tables, L0_rec_Wz, L0_rec_bz, L0_rec_Wpi, L0_rec_bpi, L0_rec_Wpo, L0_rec_bpo, L0_rec_B1, L0_rec_W1, L0_rec_b1, L0_rec_W2, L0_rec_b2, L0_rec_W3, L0_rec_b3):
    import jax
    import jax.numpy as jnp

    def _L0_rec_ref(sparse, dense, tables, Wz, bz, Wpi, bpi, Wpo, bpo, B1, W1, b1, W2, b2, W3, b3):
        import jax, jax.numpy as jnp
        import numpy as np
        B, F, V, E, D1, DD, L2 = (512, 32, 6250, 64, 256, 16, 128)
        emb = tables[jnp.arange(F)[None, :], sparse]
        Lz = jnp.einsum('bfe,dfe->bd', emb, Wz) + bz
        inner = jnp.einsum('bie,bje->bij', emb, emb)
        Lp_inner = jnp.einsum('bij,dij->bd', inner, Wpi) + bpi
        s = emb.sum(axis=1)
        outer = s[:, :, None] * s[:, None, :]
        Lp_outer = jnp.einsum('bij,dij->bd', outer, Wpo) + bpo
        L1 = Lz + Lp_inner + Lp_outer + B1
        deep_x = jnp.concatenate([L1, dense], axis=1)
        h = jnp.tanh(deep_x @ W1 + b1)
        h = jnp.tanh(h @ W2 + b2)
        out = (h @ W3 + b3)[:, 0]
        return out
    y = _L0_rec_ref(r_sparse, r_dense, L0_rec_tables, L0_rec_Wz, L0_rec_bz, L0_rec_Wpi, L0_rec_bpi, L0_rec_Wpo, L0_rec_bpo, L0_rec_B1, L0_rec_W1, L0_rec_b1, L0_rec_W2, L0_rec_b2, L0_rec_W3, L0_rec_b3)
    return y

_drawn_inputs = setup_inputs


def setup_inputs(seed=0):
    import zlib

    import numpy as np

    out = dict(_drawn_inputs(seed))
    spreads = {'L0_rec_bz': (0.0, 0.1),
     'L0_rec_bpi': (0.0, 0.1),
     'L0_rec_bpo': (0.0, 0.1),
     'L0_rec_b1': (0.0, 0.1),
     'L0_rec_b2': (0.0, 0.1)}
    factors = {}
    for name, (base, spread) in spreads.items():
        noise = np.random.default_rng([zlib.crc32(name.encode()), seed]).standard_normal(out[name].shape)
        drawn = base * np.exp(spread * noise) if base else spread * noise
        out[name] = jnp.asarray(drawn.astype(out[name].dtype))
    for name, factor in factors.items():
        out[name] = (out[name] * factor).astype(out[name].dtype)
    return out
```

```python
from contextlib import ExitStack

import concourse.bass as bass
from concourse import mybir

ALU = mybir.AluOpType
ACT = mybir.ActivationFunctionType
F32 = mybir.dt.float32
I32 = mybir.dt.int32
AX_X = mybir.AxisListType.X

P = 128
NQ = 4
DMA_INC = 16


def build_rec(nc, sparse_t, dense_t, tables, wz_t, wpi_t, wpo_a, wpo_b, w1, w2, w3,
              bias_cols, b3, ident, field_base, out):
    F, V, E = tables.shape
    B = out.shape[0]
    D1 = w1.shape[1]
    L2 = w2.shape[1]
    DD = w1.shape[0] - D1
    TB = P
    NT = B // TB
    SPC = P // F
    CALLS = TB // SPC
    CQ = CALLS // NQ
    PQ = CQ // 2
    SQ = PQ * SPC
    HALF = TB // 2
    FH = F // 2
    JW = F // 4
    NR = E // 4 + 1
    DH = D1 // P
    assert E == 64 and F == 32 and DH == 2 and L2 == P and NT % 2 == 0
    rows = tables.rearrange("f v e -> (f v) e")

    with ExitStack() as ctx:
        def sb(name, shape, dt=F32):
            return ctx.enter_context(nc.sbuf_tensor(name, shape, dt))

        def pb(name, shape):
            return ctx.enter_context(nc.psum_tensor(name, shape, F32))

        def sem(name):
            return ctx.enter_context(nc.semaphore(name))

        id_sb = sb("id_sb", [P, P])
        base_sb = sb("base_sb", [P, 1], I32)
        wz_sb = sb("wz_sb", [P, FH, D1])
        wpi_sb = sb("wpi_sb", [P, JW, D1])
        wpo_sb = sb("wpo_sb", [P, NR, D1])
        wpo_mirror = sb("wpo_mirror", [P, NR, D1])
        w1_sb = sb("w1_sb", [P, DH, D1])
        w1_dense = sb("w1_dense", [DD, D1])
        w2_sb = sb("w2_sb", [P, DH, L2])
        w3_sb = sb("w3_sb", [P, 1])
        bias_sb = sb("bias_sb", [P, bias_cols.shape[1]])
        b3_sb = sb("b3_sb", [1, 1])
        l1_bias = sb("l1_bias", [P, DH])
        l1_half = sb("l1_half", [P, 2, DH])
        dense_sb = sb("dense_sb", [DD, B])
        y_sb = sb("y_sb", [1, B])
        tanh_warm = sb("tanh_warm", [P, 1])
        raw = sb("raw", [P, NT * CALLS], I32)
        wrap = sb("wrap", [P, NT * CALLS])
        clamped = sb("clamped", [P, NT * CALLS], I32)
        row_no = sb("row_no", [P, 2, CALLS], I32)
        pool_scratch = sb("pool_scratch", [P, 1], I32)
        emb = sb("emb", [P, 2, CALLS, E])
        embT = sb("embT", [P, NQ, PQ * P])
        linT = sb("linT", [P, 2, FH, TB])
        gram = sb("gram", [P, 2, JW, TB])
        s_half = sb("s_half", [P, HALF])
        s_twice = sb("s_twice", [P, TB])
        s_rot = sb("s_rot", [P, NR, TB])
        pairs = sb("pairs", [P, NR, TB])
        l1 = sb("l1", [P, DH, TB])
        h1 = sb("h1", [P, DH, TB])
        h2 = sb("h2", [P, TB])
        s_dram = nc.dram_tensor("s_scratch", [P, TB], F32, kind="Internal").ap()

        ps_t = pb("ps_t", [P, 2, PQ * P])
        ps_g = pb("ps_g", [P, 2, CQ, P])
        ps_a = pb("ps_a", [P, 4, TB])
        ps_b = pb("ps_b", [P, 4, TB])
        ps_l1 = [ps_a[:, 0, :], ps_b[:, 0, :]]
        ps_h1 = [ps_a[:, 1, :], ps_a[:, 2, :]]
        ps_h2 = ps_b[:, 1, :]
        ps_y = ps_b[0:1, 2, :]

        raw_loaded = sem("raw_loaded")
        raw_rest_loaded = sem("raw_rest_loaded")
        base_loaded = sem("base_loaded")
        id_loaded = sem("id_loaded")
        wz_loaded = sem("wz_loaded")
        wpi_loaded = sem("wpi_loaded")
        wpo_loaded = sem("wpo_loaded")
        mlp_loaded = sem("mlp_loaded")
        bias_loaded = sem("bias_loaded")
        rows_step = sem("rows_step")
        bias_step = sem("bias_step")
        wpo_summed = sem("wpo_summed")
        row_no_ready = sem("row_no_ready")
        pool_gate = sem("pool_gate")
        gathered = [[sem(f"gathered{b}{j}") for j in range(NQ)] for b in range(2)]
        transposed = sem("transposed")
        embT_ready = sem("embT_ready")
        lin_ready = sem("lin_ready")
        sum_ready = sem("sum_ready")
        gram_done = sem("gram_done")
        gram_lo_moved = sem("gram_lo_moved")
        gram_hi_moved = sem("gram_hi_moved")
        s_ready = sem("s_ready")
        s_stored = sem("s_stored")
        rot_loaded = sem("rot_loaded")
        pairs_ready = sem("pairs_ready")
        l1_done = sem("l1_done")
        l1_ready = sem("l1_ready")
        layer1_done = sem("layer1_done")
        h1_ready = sem("h1_ready")
        layer2_done = sem("layer2_done")
        h2_ready = sem("h2_ready")
        layer3_done = sem("layer3_done")
        y_ready = sem("y_ready")
        out_stored = sem("out_stored")

        def quarter(t, j):
            return t * NQ + (j + 1)

        block = ctx.enter_context(nc.Block())

        @block.sync
        def _(sp):
            sp.dma_start(raw[:, 0:CALLS], sparse_t[:, 0:CALLS]).then_inc(raw_loaded, DMA_INC)
            sp.dma_start(base_sb[:], field_base).then_inc(base_loaded, DMA_INC)
            sp.dma_start(raw[:, CALLS:], sparse_t[:, CALLS:]).then_inc(raw_rest_loaded, DMA_INC)
            sp.dma_start(id_sb[:], ident).then_inc(id_loaded, DMA_INC)
            sp.dma_start(bias_sb[:], bias_cols).then_inc(bias_loaded, DMA_INC)
            sp.dma_start(wz_sb[:], wz_t).then_inc(wz_loaded, DMA_INC)
            sp.dma_start(wpi_sb[:], wpi_t).then_inc(wpi_loaded, DMA_INC)
            sp.dma_start(wpo_sb[:], wpo_a).then_inc(wpo_loaded, DMA_INC)
            sp.dma_start(wpo_mirror[:], wpo_b).then_inc(wpo_loaded, DMA_INC)
            sp.dma_start(w1_sb[:], w1[0:D1, :].rearrange("(c p) n -> p c n", p=P)).then_inc(mlp_loaded, DMA_INC)
            sp.dma_start(w1_dense[:], w1[D1:, :]).then_inc(mlp_loaded, DMA_INC)
            sp.dma_start(w2_sb[:], w2.rearrange("(c p) n -> p c n", p=P)).then_inc(mlp_loaded, DMA_INC)
            sp.dma_start(w3_sb[:], w3).then_inc(mlp_loaded, DMA_INC)
            sp.dma_start(dense_sb[:], dense_t).then_inc(mlp_loaded, DMA_INC)
            sp.dma_start(b3_sb[:], b3.rearrange("(a n) -> a n", a=1)).then_inc(mlp_loaded, DMA_INC)

            def rotate(t):
                sp.wait_ge(s_ready, t + 1)
                sp.dma_start(s_dram, s_twice[:]).then_inc(s_stored, DMA_INC)
                sp.wait_ge(s_stored, (t + 1) * DMA_INC)
                for h in range(2):
                    n = NR - h
                    src = bass.AP(tensor=s_dram.tensor, offset=h * TB,
                                  ap=[[TB, E], [2 * TB, n], [1, TB]])
                    sp.dma_start(s_rot[h * E:(h + 1) * E, 0:n, :], src).then_inc(rot_loaded, DMA_INC)

            with sp.Fori(0, NT) as t:
                rotate(t)
            sp.wait_ge(y_ready, 1 + NT)
            sp.dma_start(out.rearrange("(a n) -> a n", a=1), y_sb[:]).then_inc(out_stored, DMA_INC)
            sp.wait_ge(out_stored, DMA_INC)

        @block.gpsimd
        def _(pool):
            pool.wait_ge(base_loaded, DMA_INC)
            pool.wait_ge(rows_step, 3)

            def gather(t, parity, first=False):
                if not first:
                    pool.wait_ge(transposed, quarter(t - 2, NQ - 1))
                nc.gpsimd.tensor_tensor(row_no[:, parity, :], clamped[:, bass.ds(t * CALLS, CALLS)],
                                        base_sb[:, 0:1].to_broadcast([P, CALLS]), ALU.add).then_inc(row_no_ready, 1)
                pool.wait_ge(row_no_ready, t + 1)
                nc.gpsimd.tensor_tensor(pool_scratch[:], base_sb[:], base_sb[:], ALU.add).then_inc(pool_gate, 1)
                for c in range(CALLS):
                    nc.gpsimd.indirect_dma_start(
                        out=emb[:, parity, c, :], out_offset=None, in_=rows,
                        in_offset=bass.IndirectOffsetOnAxis(ap=row_no[:, parity, c:c + 1], axis=0),
                    ).then_inc(gathered[parity][c // CQ], DMA_INC)

            gather(0, 0, first=True)
            pool.wait_ge(rows_step, 6)
            gather(1, 1, first=True)
            with pool.Fori(0, NT // 2 - 1) as u:
                gather(u * 2 + 2, 0)
                gather(u * 2 + 3, 1)

        @block.tensor
        def _(pe):
            def transposes(t, parity, use, j):
                pe.wait_ge(gathered[parity][j], use * (CQ * DMA_INC))
                if not (isinstance(t, int) and t == 0 and j < 2):
                    pe.wait_ge(embT_ready, quarter(t, j - 2))
                for k in range(PQ):
                    c = j * CQ + 2 * k
                    mm = nc.tensor.transpose(ps_t[:, j % 2, k * P:(k + 1) * P],
                                             emb[:, parity, c:c + 2, :].rearrange("p c e -> p (c e)"), id_sb[:])
                mm.then_inc(transposed, 1)

            def grams(t, j):
                pe.wait_ge(embT_ready, quarter(t, j))
                if not (isinstance(t, int) and t == 0 and j < 2):
                    pe.wait_ge(gram_lo_moved, quarter(t, j - 2))
                    pe.wait_ge(gram_hi_moved, quarter(t, j - 2))
                for k in range(PQ):
                    for h in range(2):
                        x = embT[h * E:(h + 1) * E, j, k * P:(k + 1) * P]
                        mm = nc.tensor.matmul(ps_g[:, j % 2, h * PQ + k, :], x, x, start=True, stop=True)
                mm.then_inc(gram_done, 1)

            def contract_linear(t, parity):
                pe.wait_ge(lin_ready, quarter(t, NQ - 1))
                for d in range(DH):
                    if d == 1:
                        pe.wait_ge(y_ready, t + 1)
                    for f in range(FH):
                        nc.tensor.matmul(ps_l1[d], wz_sb[:, f, d * P:(d + 1) * P], linT[:, parity, f, :],
                                         start=(f == 0), stop=False)

            def contract_inner(t, parity):
                pe.wait_ge(gram_lo_moved, quarter(t, NQ - 1))
                pe.wait_ge(gram_hi_moved, quarter(t, NQ - 1))
                for d in range(DH):
                    for j in range(JW):
                        nc.tensor.matmul(ps_l1[d], wpi_sb[:, j, d * P:(d + 1) * P], gram[:, parity, j, :],
                                         start=False, stop=False)

            def contract_outer(t, d):
                if d == 0:
                    pe.wait_ge(pairs_ready, t + 1)
                for c in range(NR):
                    k = P if c < NR - 1 else E
                    mm = nc.tensor.matmul(ps_l1[d], wpo_sb[0:k, c, d * P:(d + 1) * P], pairs[0:k, c, :],
                                          start=False, stop=(c == NR - 1))
                if d == DH - 1:
                    mm.then_inc(l1_done, 1)

            def layer1(t):
                pe.wait_ge(l1_ready, t + 1)
                for m in range(DH):
                    for k in range(DH):
                        nc.tensor.matmul(ps_h1[m], w1_sb[:, k, m * P:(m + 1) * P], l1[:, k, :],
                                         start=(k == 0), stop=False)
                    mm = nc.tensor.matmul(ps_h1[m], w1_dense[:, m * P:(m + 1) * P],
                                          dense_sb[:, bass.ds(t * TB, TB)], start=False, stop=True)
                mm.then_inc(layer1_done, 1)

            def layer2(t):
                pe.wait_ge(h1_ready, t + 1)
                for k in range(DH):
                    mm = nc.tensor.matmul(ps_h2, w2_sb[:, k, :], h1[:, k, :], start=(k == 0), stop=(k == DH - 1))
                mm.then_inc(layer2_done, 1)

            def layer3(t):
                pe.wait_ge(h2_ready, t + 1)
                nc.tensor.matmul(ps_y, w3_sb[:], h2[:], start=True, stop=True).then_inc(layer3_done, 1)

            def step(t, parity, use, contract=True):
                prev = t - 1
                transposes(t, parity, use, 0)
                if contract:
                    contract_linear(prev, 1 - parity)
                grams(t, 0)
                transposes(t, parity, use, 1)
                if contract:
                    contract_inner(prev, 1 - parity)
                    contract_outer(prev, 0)
                grams(t, 1)
                transposes(t, parity, use, 2)
                if contract:
                    contract_outer(prev, 1)
                grams(t, 2)
                transposes(t, parity, use, 3)
                if contract:
                    layer1(prev)
                grams(t, 3)
                if contract:
                    layer2(prev)
                    layer3(prev)

            pe.wait_ge(id_loaded, DMA_INC)
            step(0, 0, 1, contract=False)
            pe.wait_ge(wz_loaded, DMA_INC)
            pe.wait_ge(wpi_loaded, DMA_INC)
            pe.wait_ge(wpo_summed, 2)
            pe.wait_ge(mlp_loaded, 6 * DMA_INC)
            with pe.Fori(0, NT // 2 - 1) as u:
                step(u * 2 + 1, 1, u + 1)
                step(u * 2 + 2, 0, u + 2)
            step(NT - 1, 1, NT // 2)
            t = NT - 1
            contract_linear(t, 1)
            contract_inner(t, 1)
            contract_outer(t, 0)
            contract_outer(t, 1)
            layer1(t)
            layer2(t)
            layer3(t)

        def move_gram(copy, parity, j, quadrants):
            for q in quadrants:
                for r in range(4):
                    for_halves = ps_g[q * F:(q + 1) * F, j % 2, :, q * F + r * JW:q * F + (r + 1) * JW]
                    dst = gram[r * F:(r + 1) * F, parity, :, :].rearrange(
                        "p j (h n q) -> p q h n j", h=2, q=SPC)[:, q, :, j * PQ:(j + 1) * PQ, :]
                    last = copy(dst, for_halves.rearrange("p (h n) j -> p h n j", h=2))
            return last

        @block.vector
        def _(dve):
            def clamp_rows(lo, hi, done):
                nc.vector.tensor_scalar(wrap[:, lo:hi], raw[:, lo:hi], 0.0, float(V),
                                        ALU.is_lt, ALU.mult).then_inc(rows_step, 1)
                dve.wait_ge(rows_step, done + 1)
                nc.vector.tensor_tensor(wrap[:, lo:hi], raw[:, lo:hi], wrap[:, lo:hi],
                                        ALU.add).then_inc(rows_step, 1)
                dve.wait_ge(rows_step, done + 2)
                nc.vector.tensor_scalar(clamped[:, lo:hi], wrap[:, lo:hi], 0.0, float(V - 1),
                                        ALU.max, ALU.min).then_inc(rows_step, 1)

            dve.wait_ge(raw_loaded, DMA_INC)
            clamp_rows(0, CALLS, 0)
            dve.wait_ge(raw_rest_loaded, DMA_INC)
            clamp_rows(CALLS, NT * CALLS, 3)
            dve.wait_ge(bias_loaded, DMA_INC)
            nc.vector.tensor_tensor(l1_half[:, 0, :], bias_sb[:, 0:DH], bias_sb[:, DH:2 * DH],
                                    ALU.add).then_inc(bias_step, 1)
            nc.vector.tensor_tensor(l1_half[:, 1, :], bias_sb[:, 2 * DH:3 * DH], bias_sb[:, 3 * DH:4 * DH],
                                    ALU.add).then_inc(bias_step, 1)
            dve.wait_ge(bias_step, 2)
            nc.vector.tensor_tensor(l1_bias[:], l1_half[:, 0, :], l1_half[:, 1, :], ALU.add).then_inc(bias_step, 1)

            def quarter_in(t, parity, j):
                dve.wait_ge(transposed, quarter(t, j))
                if not (isinstance(t, int) and t == 0):
                    dve.wait_ge(lin_ready, quarter(t - 1, j))
                nc.vector.tensor_copy(embT[:, j, :], ps_t[:, j % 2, :]).then_inc(embT_ready, 1)
                dve.wait_ge(embT_ready, quarter(t, j))
                nc.vector.reduce_sum(s_half[:, j * SQ:(j + 1) * SQ],
                                     embT[:, j, :].rearrange("p (s f) -> p s f", f=F), AX_X).then_inc(sum_ready, 1)

            def quarter_gram(t, parity, j):
                dve.wait_ge(gram_done, quarter(t, j))
                move_gram(nc.vector.tensor_copy, parity, j, (0, 1)).then_inc(gram_lo_moved, 1)

            def spread_sums(t):
                dve.wait_ge(sum_ready, quarter(t, NQ - 1))
                for h in range(2):
                    for g in range(2):
                        last = nc.vector.tensor_copy(s_twice[g * E:(g + 1) * E, h * HALF:(h + 1) * HALF],
                                                     s_half[h * E:(h + 1) * E, :])
                last.then_inc(s_ready, 1)

            def form_pairs(t):
                dve.wait_ge(rot_loaded, (t * 2 + 2) * DMA_INC)
                nc.vector.tensor_tensor(pairs[:, 0:NR - 1, :], s_rot[:, 0:NR - 1, :],
                                        s_twice[:].unsqueeze(1).to_broadcast([P, NR - 1, TB]), ALU.mult)
                nc.vector.tensor_tensor(pairs[0:E, NR - 1, :], s_rot[0:E, NR - 1, :], s_twice[0:E, :],
                                        ALU.mult).then_inc(pairs_ready, 1)

            def bias_l1(t):
                dve.wait_ge(l1_done, t + 1)
                for d in range(DH):
                    last = nc.vector.tensor_scalar(l1[:, d, :], ps_l1[d], l1_bias[:, d:d + 1], None, ALU.add)
                last.then_inc(l1_ready, 1)

            def step(t, parity, contract=True):
                prev = t - 1
                quarter_in(t, parity, 0)
                quarter_gram(t, parity, 0)
                quarter_in(t, parity, 1)
                if contract:
                    form_pairs(prev)
                quarter_gram(t, parity, 1)
                quarter_in(t, parity, 2)
                if contract:
                    bias_l1(prev)
                quarter_gram(t, parity, 2)
                quarter_in(t, parity, 3)
                spread_sums(t)
                quarter_gram(t, parity, 3)

            step(0, 0, contract=False)
            dve.wait_ge(wpo_loaded, 2 * DMA_INC)
            nc.vector.tensor_tensor(wpo_sb[0:E, 1:NR - 1, :], wpo_sb[0:E, 1:NR - 1, :],
                                    wpo_mirror[0:E, 1:NR - 1, :], ALU.add).then_inc(wpo_summed, 1)
            nc.vector.tensor_tensor(wpo_sb[E:P, 0:NR - 1, :], wpo_sb[E:P, 0:NR - 1, :],
                                    wpo_mirror[E:P, 0:NR - 1, :], ALU.add).then_inc(wpo_summed, 1)
            dve.wait_ge(bias_step, 3)
            with dve.Fori(0, NT // 2 - 1) as u:
                step(u * 2 + 1, 1)
                step(u * 2 + 2, 0)
            step(NT - 1, 1)
            form_pairs(NT - 1)
            bias_l1(NT - 1)

        @block.scalar
        def _(act):
            b1_col = [bias_sb[:, 4 * DH + m:4 * DH + m + 1] for m in range(DH)]
            b2_col = bias_sb[:, 5 * DH:5 * DH + 1]

            def quarter_linear(t, parity, j):
                act.wait_ge(embT_ready, quarter(t, j))
                for h in range(2):
                    for g in range(2):
                        src = embT[h * E:(h + 1) * E, j, :].rearrange(
                            "p (s g f) -> p g f s", g=2, f=FH)[:, g]
                        s0 = h * HALF + j * SQ
                        last = nc.scalar.copy(linT[g * E:(g + 1) * E, parity, :, s0:s0 + SQ], src)
                last.then_inc(lin_ready, 1)

            def quarter_gram(t, parity, j):
                act.wait_ge(gram_done, quarter(t, j))
                move_gram(nc.scalar.copy, parity, j, (2, 3)).then_inc(gram_hi_moved, 1)

            def tanh1(t):
                act.wait_ge(layer1_done, t + 1)
                for m in range(DH):
                    last = nc.scalar.activation(h1[:, m, :], ps_h1[m], ACT.Tanh, bias=b1_col[m])
                last.then_inc(h1_ready, 1)

            def tanh2(t):
                act.wait_ge(layer2_done, t + 1)
                nc.scalar.activation(h2[:], ps_h2, ACT.Tanh, bias=b2_col).then_inc(h2_ready, 1)

            def store_y(t):
                act.wait_ge(layer3_done, t + 1)
                nc.scalar.activation(y_sb[:, bass.ds(t * TB, TB)], ps_y, ACT.Identity,
                                     bias=b3_sb[:, 0:1]).then_inc(y_ready, 1)

            def step(t, parity, contract=True):
                prev = t - 1
                for j in range(NQ):
                    quarter_linear(t, parity, j)
                    if contract and j == NQ - 1:
                        tanh1(prev)
                    quarter_gram(t, parity, j)
                if contract:
                    tanh2(prev)
                    store_y(prev)

            act.wait_ge(id_loaded, DMA_INC)
            nc.scalar.activation(tanh_warm[:], id_sb[:, 0:1], ACT.Tanh).then_inc(y_ready, 1)
            step(0, 0, contract=False)
            act.wait_ge(bias_loaded, DMA_INC)
            act.wait_ge(mlp_loaded, 6 * DMA_INC)
            with act.Fori(0, NT // 2 - 1) as u:
                step(u * 2 + 1, 1)
                step(u * 2 + 2, 0)
            step(NT - 1, 1)
            tanh1(NT - 1)
            tanh2(NT - 1)
            store_y(NT - 1)


def kernel(r_dense, r_sparse, L0_rec_tables, L0_rec_Wz, L0_rec_bz, L0_rec_Wpi, L0_rec_bpi, L0_rec_Wpo,
           L0_rec_bpo, L0_rec_B1, L0_rec_W1, L0_rec_b1, L0_rec_W2, L0_rec_b2, L0_rec_W3, L0_rec_b3):
    import numpy as np
    import concourse.bacc as bacc
    from concourse import mybir as mb
    from concourse.bass_utils import run_bass_kernel_spmd

    a = {k: np.asarray(v) for k, v in dict(
        dense=r_dense, sparse=r_sparse, tables=L0_rec_tables, wz=L0_rec_Wz, wpi=L0_rec_Wpi, wpo=L0_rec_Wpo,
        w1=L0_rec_W1, w2=L0_rec_W2, w3=L0_rec_W3, bz=L0_rec_bz, bpi=L0_rec_bpi, bpo=L0_rec_bpo,
        B1=L0_rec_B1, b1=L0_rec_b1, b2=L0_rec_b2, b3=L0_rec_b3).items()}
    B, F = a["sparse"].shape
    D1, _, E = a["wz"].shape
    V = a["tables"].shape[1]

    sparse = a["sparse"].reshape(B // P, 2, F // 2, P // F, F).transpose(3, 4, 0, 2, 1).reshape(P, -1)
    wz = a["wz"].reshape(D1, 2, F // 2, E).transpose(1, 3, 2, 0).reshape(P, F // 2, D1)
    wpi = a["wpi"].reshape(D1, F, 4, F // 4).transpose(2, 1, 3, 0).reshape(P, F // 4, D1)
    p = np.arange(E)
    k = np.arange(2)[:, None, None] + 2 * np.arange(E // 4 + 1)[None, None, :]
    q = (p[None, :, None] + k) % E
    pp = np.broadcast_to(p[None, :, None], q.shape)
    wpo_a = a["wpo"][:, pp, q].transpose(1, 2, 3, 0).reshape(P, -1, D1)
    wpo_b = a["wpo"][:, q, pp].transpose(1, 2, 3, 0).reshape(P, -1, D1)
    columns = lambda v: v.reshape(-1, P).T
    bias_cols = np.concatenate([columns(a[n]) for n in ("bz", "bpi", "bpo", "B1", "b1", "b2")], axis=1)

    arrays = {
        "sparse_t": sparse, "dense_t": a["dense"].T, "tables": a["tables"], "wz_t": wz, "wpi_t": wpi,
        "wpo_a": wpo_a, "wpo_b": wpo_b, "w1": a["w1"], "w2": a["w2"], "w3": a["w3"],
        "bias_cols": bias_cols, "b3": a["b3"], "ident": np.eye(P, dtype=np.float32),
        "field_base": (np.arange(P) % F * V).astype(np.int32).reshape(P, 1),
    }
    arrays = {n: np.ascontiguousarray(v) for n, v in arrays.items()}
    nc = bacc.Bacc("TRN2", target_bir_lowering=False, num_devices=1)
    args = [nc.dram_tensor(n, v.shape, mb.dt.from_np(v.dtype), kind="ExternalInput").ap() for n, v in arrays.items()]
    args.append(nc.dram_tensor("out", (B,), F32, kind="ExternalOutput").ap())
    build_rec(nc, *args)
    result = run_bass_kernel_spmd(nc, [arrays], core_ids=[0])
    return result.results[0]["out"]
```

```python
from contextlib import ExitStack

import concourse.bass as bass
from concourse import mybir

ALU = mybir.AluOpType
ACT = mybir.ActivationFunctionType
F32 = mybir.dt.float32
I32 = mybir.dt.int32
AX_X = mybir.AxisListType.X

P = 128
NQ = 4
DMA_INC = 16


def build_rec(nc, sparse_t, dense_t, tables, wz_t, wpi_t, wpo_a, wpo_b, w1, w2, w3,
              bias_cols, b3, ident, field_base, out):
    F, V, E = tables.shape
    B = out.shape[0]
    D1 = w1.shape[1]
    L2 = w2.shape[1]
    DD = w1.shape[0] - D1
    TB = P
    NT = B // TB
    SPC = P // F
    CALLS = TB // SPC
    CQ = CALLS // NQ
    PQ = CQ // 2
    SQ = PQ * SPC
    FH = F // 2
    JW = F // 4
    NR = E // 4 + 1
    DH = D1 // P
    assert E == 64 and F == 32 and DH == 2 and L2 == P and NT % 2 == 0
    rows = tables.rearrange("f v e -> (f v) e")

    with ExitStack() as ctx:
        def sb(name, shape, dt=F32):
            return ctx.enter_context(nc.sbuf_tensor(name, shape, dt))

        def pb(name, shape):
            return ctx.enter_context(nc.psum_tensor(name, shape, F32))

        def sem(name):
            return ctx.enter_context(nc.semaphore(name))

        id_sb = sb("id_sb", [P, P])
        base_sb = sb("base_sb", [P, 1])
        wz_sb = sb("wz_sb", [P, FH, D1])
        wpi_sb = sb("wpi_sb", [P, JW, D1])
        wpo_sb = sb("wpo_sb", [P, NR, D1])
        wpo_mirror = sb("wpo_mirror", [P, NR, D1])
        w1_sb = sb("w1_sb", [P, DH, D1])
        w1_dense = sb("w1_dense", [DD, D1])
        w2_sb = sb("w2_sb", [P, DH, L2])
        w3_sb = sb("w3_sb", [P, 1])
        bias_sb = sb("bias_sb", [P, bias_cols.shape[1]])
        b3_sb = sb("b3_sb", [1, 1])
        l1_bias = sb("l1_bias", [P, DH])
        l1_half = sb("l1_half", [P, 2, DH])
        dense_sb = sb("dense_sb", [DD, B])
        y_sb = sb("y_sb", [1, B])
        tanh_warm = sb("tanh_warm", [P, 1])
        raw = sb("raw", [P, NT * CALLS], I32)
        bounded = sb("bounded", [P, NT * CALLS])
        from_end = sb("from_end", [P, NT * CALLS])
        rows_all = sb("rows_all", [P, NT * CALLS], I32)
        row_no = sb("row_no", [P, 2, CALLS], I32)
        pool_gate_in = sb("pool_gate_in", [P, 1], I32)
        pool_gate_out = sb("pool_gate_out", [P, 1], I32)
        emb = sb("emb", [P, 2, CALLS, E])
        embT = sb("embT", [P, NQ, PQ * P])
        linT = sb("linT", [P, 2, FH, TB])
        gram = sb("gram", [P, 2, JW, TB])
        s_half = sb("s_half", [P, NQ, SQ])
        s_twice = sb("s_twice", [P, TB])
        s_rot = sb("s_rot", [P, NR, TB])
        pairs = sb("pairs", [P, NR, TB])
        l1 = sb("l1", [P, DH, TB])
        h1 = sb("h1", [P, DH, TB])
        h2 = sb("h2", [P, TB])
        s_dram = nc.dram_tensor("s_scratch", [P, TB], F32, kind="Internal").ap()

        ps_t = pb("ps_t", [P, 2, PQ * P])
        ps_g = pb("ps_g", [P, 2, CQ, P])
        ps_l1 = pb("ps_l1", [P, 4, TB])
        ps_mlp = pb("ps_mlp", [P, 4, TB])
        ps_h2 = ps_mlp[:, DH, :]
        ps_y = ps_mlp[0:1, DH + 1, :]

        raw_loaded = sem("raw_loaded")
        raw_rest_loaded = sem("raw_rest_loaded")
        base_loaded = sem("base_loaded")
        id_loaded = sem("id_loaded")
        wz_loaded = sem("wz_loaded")
        wpi_loaded = sem("wpi_loaded")
        wpo_loaded = sem("wpo_loaded")
        mlp_loaded = sem("mlp_loaded")
        bias_loaded = sem("bias_loaded")
        rows_step = sem("rows_step")
        bias_step = sem("bias_step")
        wpo_summed = sem("wpo_summed")
        row_no_ready = sem("row_no_ready")
        gate_cleared = sem("gate_cleared")
        gathered = [[sem(f"gathered{b}{j}") for j in range(NQ)] for b in range(2)]
        transposed = sem("transposed")
        embT_ready = sem("embT_ready")
        lin_ready = sem("lin_ready")
        sum_ready = sem("sum_ready")
        gram_done = sem("gram_done")
        gram_lo_moved = sem("gram_lo_moved")
        gram_hi_moved = sem("gram_hi_moved")
        s_ready = sem("s_ready")
        s_stored = sem("s_stored")
        rot_loaded = sem("rot_loaded")
        pairs_ready = sem("pairs_ready")
        l1_done = sem("l1_done")
        l1_ready = sem("l1_ready")
        layer1_done = sem("layer1_done")
        h1_ready = sem("h1_ready")
        layer2_done = sem("layer2_done")
        h2_ready = sem("h2_ready")
        layer3_done = sem("layer3_done")
        y_ready = sem("y_ready")
        out_stored = sem("out_stored")

        def quarter(t, j):
            return t * NQ + (j + 1)

        block = ctx.enter_context(nc.Block())

        @block.sync
        def _(sp):
            sp.dma_start(raw[:, 0:CALLS], sparse_t[:, 0:CALLS]).then_inc(raw_loaded, DMA_INC)
            sp.dma_start(base_sb[:], field_base).then_inc(base_loaded, DMA_INC)
            sp.dma_start(raw[:, CALLS:], sparse_t[:, CALLS:]).then_inc(raw_rest_loaded, DMA_INC)
            sp.dma_start(id_sb[:], ident).then_inc(id_loaded, DMA_INC)
            sp.dma_start(bias_sb[:], bias_cols).then_inc(bias_loaded, DMA_INC)
            sp.dma_start(wz_sb[:], wz_t).then_inc(wz_loaded, DMA_INC)
            sp.dma_start(wpi_sb[:], wpi_t).then_inc(wpi_loaded, DMA_INC)
            sp.dma_start(wpo_sb[:], wpo_a).then_inc(wpo_loaded, DMA_INC)
            sp.dma_start(wpo_mirror[:], wpo_b).then_inc(wpo_loaded, DMA_INC)
            sp.dma_start(w1_sb[:], w1[0:D1, :].rearrange("(c p) n -> p c n", p=P)).then_inc(mlp_loaded, DMA_INC)
            sp.dma_start(w1_dense[:], w1[D1:, :]).then_inc(mlp_loaded, DMA_INC)
            sp.dma_start(w2_sb[:], w2.rearrange("(c p) n -> p c n", p=P)).then_inc(mlp_loaded, DMA_INC)
            sp.dma_start(w3_sb[:], w3).then_inc(mlp_loaded, DMA_INC)
            sp.dma_start(dense_sb[:], dense_t).then_inc(mlp_loaded, DMA_INC)
            sp.dma_start(b3_sb[:], b3.rearrange("(a n) -> a n", a=1)).then_inc(mlp_loaded, DMA_INC)

            with sp.Fori(0, NT) as t:
                sp.wait_ge(s_ready, t + 1)
                sp.dma_start(s_dram, s_twice[:]).then_inc(s_stored, DMA_INC)
                sp.wait_ge(s_stored, (t + 1) * DMA_INC)
                for h in range(2):
                    chunks = NR - h
                    src = bass.AP(tensor=s_dram.tensor, offset=h * TB,
                                  ap=[[TB, E], [2 * TB, chunks], [1, TB]])
                    sp.dma_start(s_rot[h * E:(h + 1) * E, 0:chunks, :], src).then_inc(rot_loaded, DMA_INC)
            sp.wait_ge(y_ready, 1 + NT)
            sp.dma_start(out.rearrange("(a n) -> a n", a=1), y_sb[:]).then_inc(out_stored, DMA_INC)
            sp.wait_ge(out_stored, DMA_INC)

        @block.gpsimd
        def _(pool):
            def gather(parity):
                for c in range(CALLS):
                    nc.gpsimd.indirect_dma_start(
                        out=emb[:, parity, c, :], out_offset=None, in_=rows,
                        in_offset=bass.IndirectOffsetOnAxis(ap=row_no[:, parity, c:c + 1], axis=0),
                    ).then_inc(gathered[parity][c // CQ], DMA_INC)

            def gather_next(t, parity):
                pool.wait_ge(row_no_ready, t + 1)
                nc.gpsimd.tensor_tensor(pool_gate_out[:], pool_gate_in[:], pool_gate_in[:],
                                        ALU.add).then_inc(gate_cleared, 1)
                gather(parity)

            nc.gpsimd.memset(pool_gate_in[:], 0).then_inc(gate_cleared, 1)
            pool.wait_ge(gate_cleared, 1)
            pool.wait_ge(row_no_ready, 1)
            gather(0)
            pool.wait_ge(row_no_ready, 2)
            gather(1)
            with pool.Fori(0, NT // 2 - 1) as u:
                gather_next(u * 2 + 2, 0)
                gather_next(u * 2 + 3, 1)

        @block.tensor
        def _(pe):
            def transposes(t, parity, use, j):
                pe.wait_ge(gathered[parity][j], use * (CQ * DMA_INC))
                if not (isinstance(t, int) and t == 0 and j < 2):
                    pe.wait_ge(embT_ready, quarter(t, j - 2))
                for k in range(PQ):
                    c = j * CQ + 2 * k
                    mm = nc.tensor.transpose(ps_t[:, j % 2, k * P:(k + 1) * P],
                                             emb[:, parity, c:c + 2, :].rearrange("p c e -> p (c e)"), id_sb[:])
                mm.then_inc(transposed, 1)

            def grams(t, j):
                pe.wait_ge(embT_ready, quarter(t, j))
                if not (isinstance(t, int) and t == 0 and j < 2):
                    pe.wait_ge(gram_lo_moved, quarter(t, j - 2))
                    pe.wait_ge(gram_hi_moved, quarter(t, j - 2))
                for k in range(PQ):
                    for h in range(2):
                        x = embT[h * E:(h + 1) * E, j, k * P:(k + 1) * P]
                        mm = nc.tensor.matmul(ps_g[:, j % 2, h * PQ + k, :], x, x, start=True, stop=True)
                mm.then_inc(gram_done, 1)

            def contract_linear(t, parity, lo, hi):
                if lo == 0:
                    pe.wait_ge(lin_ready, quarter(t, NQ - 1))
                for i in range(lo, hi):
                    d, f = divmod(i, FH)
                    nc.tensor.matmul(ps_l1[:, d, :], wz_sb[:, f, d * P:(d + 1) * P], linT[:, parity, f, :],
                                     start=(i == 0), stop=False)

            def contract_inner(t, parity):
                pe.wait_ge(gram_lo_moved, quarter(t, NQ - 1))
                pe.wait_ge(gram_hi_moved, quarter(t, NQ - 1))
                for i in range(DH * JW):
                    d, j = divmod(i, JW)
                    nc.tensor.matmul(ps_l1[:, d, :], wpi_sb[:, j, d * P:(d + 1) * P], gram[:, parity, j, :],
                                     start=False, stop=False)

            def contract_outer(t, lo, hi):
                if lo == 0:
                    pe.wait_ge(pairs_ready, t + 1)
                for i in range(lo, hi):
                    d, c = divmod(i, NR)
                    k = P if c < NR - 1 else E
                    mm = nc.tensor.matmul(ps_l1[:, d, :], wpo_sb[0:k, c, d * P:(d + 1) * P], pairs[0:k, c, :],
                                          start=False, stop=(i == DH * NR - 1))
                if hi == DH * NR:
                    mm.then_inc(l1_done, 1)

            def layer1(t):
                pe.wait_ge(l1_ready, t + 1)
                pe.wait_ge(y_ready, t + 1)
                for m in range(DH):
                    nc.tensor.matmul(ps_mlp[:, m, :], w1_dense[:, m * P:(m + 1) * P],
                                     dense_sb[:, bass.ds(t * TB, TB)], start=True, stop=False)
                    for k in range(DH):
                        mm = nc.tensor.matmul(ps_mlp[:, m, :], w1_sb[:, k, m * P:(m + 1) * P], l1[:, k, :],
                                              start=False, stop=(k == DH - 1))
                mm.then_inc(layer1_done, 1)

            def layer2(t):
                pe.wait_ge(h1_ready, t + 1)
                for k in range(DH):
                    mm = nc.tensor.matmul(ps_h2, w2_sb[:, k, :], h1[:, k, :],
                                          start=(k == 0), stop=(k == DH - 1))
                mm.then_inc(layer2_done, 1)

            def layer3(t):
                pe.wait_ge(h2_ready, t + 1)
                nc.tensor.matmul(ps_y, w3_sb[:], h2[:], start=True, stop=True).then_inc(layer3_done, 1)

            LIN, OUT = DH * FH, DH * NR
            LIN1, OUT1 = LIN - 4, 16

            def step(t, parity, use):
                before = 1 - parity
                contract_linear(t - 1, before, 0, LIN1)
                transposes(t, parity, use, 0)
                contract_linear(t - 1, before, LIN1, LIN)
                grams(t, 0)
                contract_inner(t - 1, before)
                transposes(t, parity, use, 1)
                grams(t, 1)
                contract_outer(t - 1, 0, OUT1)
                transposes(t, parity, use, 2)
                contract_outer(t - 1, OUT1, OUT)
                grams(t, 2)
                layer1(t - 1)
                transposes(t, parity, use, 3)
                layer2(t - 1)
                grams(t, 3)
                layer3(t - 1)

            pe.wait_ge(id_loaded, DMA_INC)
            for j in range(NQ):
                transposes(0, 0, 1, j)
                grams(0, j)
            pe.wait_ge(wz_loaded, DMA_INC)
            pe.wait_ge(wpi_loaded, DMA_INC)
            pe.wait_ge(wpo_summed, 2)
            pe.wait_ge(mlp_loaded, 6 * DMA_INC)
            with pe.Fori(0, NT // 2 - 1) as u:
                step(u * 2 + 1, 1, u + 1)
                step(u * 2 + 2, 0, u + 2)
            step(NT - 1, 1, NT // 2)
            t, parity = NT - 1, 1
            contract_linear(t, parity, 0, LIN)
            contract_inner(t, parity)
            contract_outer(t, 0, OUT)
            layer1(t)
            layer2(t)
            layer3(t)

        def move_gram(copy, parity, j, quadrants):
            for q in quadrants:
                for r in range(4):
                    src = ps_g[q * F:(q + 1) * F, j % 2, :, q * F + r * JW:q * F + (r + 1) * JW]
                    dst = gram[r * F:(r + 1) * F, parity, :, 2 * j * SQ:2 * (j + 1) * SQ].rearrange(
                        "p j (m q) -> p q m j", q=SPC)[:, q]
                    last = copy(dst, src)
            return last

        @block.vector
        def _(dve):
            def bound_rows(lo, hi, done):
                nc.vector.tensor_scalar(bounded[:, lo:hi], raw[:, lo:hi], float(-V), float(V - 1),
                                        ALU.max, ALU.min).then_inc(rows_step, 1)
                dve.wait_ge(rows_step, done + 1)
                nc.vector.tensor_scalar(from_end[:, lo:hi], bounded[:, lo:hi], 0.0, float(V),
                                        ALU.is_lt, ALU.mult).then_inc(rows_step, 1)
                dve.wait_ge(rows_step, done + 2)

            def number_rows(dst, lo, hi):
                return nc.vector.scalar_tensor_tensor(
                    out=dst, in0=bounded[:, lo:hi], scalar=base_sb[:, 0:1], in1=from_end[:, lo:hi],
                    op0=ALU.add, op1=ALU.add)

            def next_rows(t, parity):
                dve.wait_ge(gate_cleared, t - 1)
                nc.vector.tensor_copy(row_no[:, parity, :],
                                      rows_all[:, bass.ds(t * CALLS, CALLS)]).then_inc(row_no_ready, 1)

            dve.wait_ge(raw_loaded, DMA_INC)
            bound_rows(0, CALLS, 0)
            dve.wait_ge(base_loaded, DMA_INC)
            number_rows(row_no[:, 0, :], 0, CALLS).then_inc(row_no_ready, 1)
            dve.wait_ge(raw_rest_loaded, DMA_INC)
            bound_rows(CALLS, NT * CALLS, 2)
            number_rows(row_no[:, 1, :], CALLS, 2 * CALLS).then_inc(row_no_ready, 1)
            number_rows(rows_all[:, CALLS:], CALLS, NT * CALLS).then_inc(rows_step, 1)
            dve.wait_ge(rows_step, 5)
            dve.wait_ge(bias_loaded, DMA_INC)
            nc.vector.tensor_tensor(l1_half[:, 0, :], bias_sb[:, 0:DH], bias_sb[:, DH:2 * DH],
                                    ALU.add).then_inc(bias_step, 1)
            nc.vector.tensor_tensor(l1_half[:, 1, :], bias_sb[:, 2 * DH:3 * DH], bias_sb[:, 3 * DH:4 * DH],
                                    ALU.add).then_inc(bias_step, 1)
            dve.wait_ge(bias_step, 2)
            nc.vector.tensor_tensor(l1_bias[:], l1_half[:, 0, :], l1_half[:, 1, :], ALU.add).then_inc(bias_step, 1)

            def quarter_in(t, j):
                dve.wait_ge(transposed, quarter(t, j))
                if not (isinstance(t, int) and t == 0):
                    dve.wait_ge(lin_ready, quarter(t - 1, j))
                nc.vector.tensor_copy(embT[:, j, :], ps_t[:, j % 2, :]).then_inc(embT_ready, 1)
                dve.wait_ge(embT_ready, quarter(t, j))
                nc.vector.reduce_sum(s_half[:, j, :], embT[:, j, :].rearrange("p (s f) -> p s f", f=F),
                                     AX_X).then_inc(sum_ready, 1)

            def quarter_gram(t, parity, j):
                dve.wait_ge(gram_done, quarter(t, j))
                move_gram(nc.vector.tensor_copy, parity, j, (0, 1)).then_inc(gram_lo_moved, 1)

            def spread_sums(t):
                dve.wait_ge(sum_ready, quarter(t, NQ - 1))
                for h in range(2):
                    for g in range(2):
                        dst = s_twice[g * E:(g + 1) * E, :].rearrange("p (j h s) -> p h j s", h=2, s=SQ)
                        last = nc.vector.tensor_copy(dst[:, h], s_half[h * E:(h + 1) * E, :, :])
                last.then_inc(s_ready, 1)

            def form_pairs(t):
                dve.wait_ge(rot_loaded, (t * 2 + 2) * DMA_INC)
                nc.vector.tensor_tensor(pairs[:, 0:NR - 1, :], s_rot[:, 0:NR - 1, :],
                                        s_twice[:].unsqueeze(1).to_broadcast([P, NR - 1, TB]), ALU.mult)
                nc.vector.tensor_tensor(pairs[0:E, NR - 1, :], s_rot[0:E, NR - 1, :], s_twice[0:E, :],
                                        ALU.mult).then_inc(pairs_ready, 1)

            def bias_l1(t):
                dve.wait_ge(l1_done, t + 1)
                for d in range(DH):
                    last = nc.vector.tensor_scalar(l1[:, d, :], ps_l1[:, d, :], l1_bias[:, d:d + 1], None, ALU.add)
                last.then_inc(l1_ready, 1)

            def step(t, parity, more=True):
                quarter_in(t, 0)
                form_pairs(t - 1)
                quarter_gram(t, parity, 0)
                quarter_in(t, 1)
                quarter_gram(t, parity, 1)
                quarter_in(t, 2)
                bias_l1(t - 1)
                quarter_gram(t, parity, 2)
                quarter_in(t, 3)
                spread_sums(t)
                if more:
                    next_rows(t + 2, parity)
                quarter_gram(t, parity, 3)

            for j in range(NQ):
                quarter_in(0, j)
                if j == NQ - 1:
                    spread_sums(0)
                    next_rows(2, 0)
                quarter_gram(0, 0, j)
            dve.wait_ge(wpo_loaded, 2 * DMA_INC)
            nc.vector.tensor_tensor(wpo_sb[0:E, 1:NR - 1, :], wpo_sb[0:E, 1:NR - 1, :],
                                    wpo_mirror[0:E, 1:NR - 1, :], ALU.add).then_inc(wpo_summed, 1)
            nc.vector.tensor_tensor(wpo_sb[E:P, 0:NR - 1, :], wpo_sb[E:P, 0:NR - 1, :],
                                    wpo_mirror[E:P, 0:NR - 1, :], ALU.add).then_inc(wpo_summed, 1)
            dve.wait_ge(bias_step, 3)
            with dve.Fori(0, NT // 2 - 2) as u:
                step(u * 2 + 1, 1)
                step(u * 2 + 2, 0)
            step(NT - 3, 1)
            step(NT - 2, 0, more=False)
            step(NT - 1, 1, more=False)
            form_pairs(NT - 1)
            bias_l1(NT - 1)

        @block.scalar
        def _(act):
            b1_col = [bias_sb[:, 4 * DH + m:4 * DH + m + 1] for m in range(DH)]
            b2_col = bias_sb[:, 5 * DH:5 * DH + 1]

            def quarter_linear(t, parity, j):
                act.wait_ge(embT_ready, quarter(t, j))
                for h in range(2):
                    for g in range(2):
                        src = embT[h * E:(h + 1) * E, j, :].rearrange(
                            "p (s g f) -> p g f s", g=2, f=FH)[:, g]
                        c0 = (2 * j + h) * SQ
                        last = nc.scalar.copy(linT[g * E:(g + 1) * E, parity, :, c0:c0 + SQ], src)
                last.then_inc(lin_ready, 1)

            def quarter_gram(t, parity, j):
                act.wait_ge(gram_done, quarter(t, j))
                move_gram(nc.scalar.copy, parity, j, (2, 3)).then_inc(gram_hi_moved, 1)

            def tanh1(t):
                act.wait_ge(layer1_done, t + 1)
                for m in range(DH):
                    last = nc.scalar.activation(h1[:, m, :], ps_mlp[:, m, :], ACT.Tanh, bias=b1_col[m])
                last.then_inc(h1_ready, 1)

            def tanh2(t):
                act.wait_ge(layer2_done, t + 1)
                nc.scalar.activation(h2[:], ps_h2, ACT.Tanh, bias=b2_col).then_inc(h2_ready, 1)

            def store_y(t):
                act.wait_ge(layer3_done, t + 1)
                nc.scalar.activation(y_sb[:, bass.ds(t * TB, TB)], ps_y, ACT.Identity,
                                     bias=b3_sb[:, 0:1]).then_inc(y_ready, 1)

            def step(t, parity):
                quarter_linear(t, parity, 0)
                quarter_gram(t, parity, 0)
                quarter_linear(t, parity, 1)
                quarter_gram(t, parity, 1)
                quarter_linear(t, parity, 2)
                quarter_gram(t, parity, 2)
                tanh1(t - 1)
                quarter_linear(t, parity, 3)
                tanh2(t - 1)
                quarter_gram(t, parity, 3)
                store_y(t - 1)

            act.wait_ge(id_loaded, DMA_INC)
            nc.scalar.activation(tanh_warm[:], id_sb[:, 0:1], ACT.Tanh).then_inc(y_ready, 1)
            for j in range(NQ):
                quarter_linear(0, 0, j)
                quarter_gram(0, 0, j)
            act.wait_ge(bias_loaded, DMA_INC)
            act.wait_ge(mlp_loaded, 6 * DMA_INC)
            with act.Fori(0, NT // 2 - 1) as u:
                step(u * 2 + 1, 1)
                step(u * 2 + 2, 0)
            step(NT - 1, 1)
            tanh1(NT - 1)
            tanh2(NT - 1)
            store_y(NT - 1)


def kernel(r_dense, r_sparse, L0_rec_tables, L0_rec_Wz, L0_rec_bz, L0_rec_Wpi, L0_rec_bpi, L0_rec_Wpo,
           L0_rec_bpo, L0_rec_B1, L0_rec_W1, L0_rec_b1, L0_rec_W2, L0_rec_b2, L0_rec_W3, L0_rec_b3):
    import numpy as np
    import concourse.bacc as bacc
    from concourse import mybir as mb
    from concourse.bass_utils import run_bass_kernel_spmd

    a = {k: np.asarray(v) for k, v in dict(
        dense=r_dense, sparse=r_sparse, tables=L0_rec_tables, wz=L0_rec_Wz, wpi=L0_rec_Wpi, wpo=L0_rec_Wpo,
        w1=L0_rec_W1, w2=L0_rec_W2, w3=L0_rec_W3, bz=L0_rec_bz, bpi=L0_rec_bpi, bpo=L0_rec_bpo,
        B1=L0_rec_B1, b1=L0_rec_b1, b2=L0_rec_b2, b3=L0_rec_b3).items()}
    B, F = a["sparse"].shape
    D1, _, E = a["wz"].shape
    V = a["tables"].shape[1]

    sparse = a["sparse"].reshape(B // P, NQ, 2, F // 2 // NQ, P // F, F)
    sparse = sparse.transpose(4, 5, 0, 1, 3, 2).reshape(P, -1)
    wz = a["wz"].reshape(D1, 2, F // 2, E).transpose(1, 3, 2, 0).reshape(P, F // 2, D1)
    wpi = a["wpi"].reshape(D1, F, 4, F // 4).transpose(2, 1, 3, 0).reshape(P, F // 4, D1)
    p = np.arange(E)
    k = np.arange(2)[:, None, None] + 2 * np.arange(E // 4 + 1)[None, None, :]
    q = (p[None, :, None] + k) % E
    pp = np.broadcast_to(p[None, :, None], q.shape)
    wpo_a = a["wpo"][:, pp, q].transpose(1, 2, 3, 0).reshape(P, -1, D1)
    wpo_b = a["wpo"][:, q, pp].transpose(1, 2, 3, 0).reshape(P, -1, D1)
    columns = lambda v: v.reshape(-1, P).T
    bias_cols = np.concatenate([columns(a[n]) for n in ("bz", "bpi", "bpo", "B1", "b1", "b2")], axis=1)

    arrays = {
        "sparse_t": sparse, "dense_t": a["dense"].T, "tables": a["tables"], "wz_t": wz, "wpi_t": wpi,
        "wpo_a": wpo_a, "wpo_b": wpo_b, "w1": a["w1"], "w2": a["w2"], "w3": a["w3"],
        "bias_cols": bias_cols, "b3": a["b3"], "ident": np.eye(P, dtype=np.float32),
        "field_base": (np.arange(P) % F * V).astype(np.float32).reshape(P, 1),
    }
    arrays = {n: np.ascontiguousarray(v) for n, v in arrays.items()}
    nc = bacc.Bacc("TRN2", target_bir_lowering=False, num_devices=1)
    args = [nc.dram_tensor(n, v.shape, mb.dt.from_np(v.dtype), kind="ExternalInput").ap() for n, v in arrays.items()]
    args.append(nc.dram_tensor("out", (B,), F32, kind="ExternalOutput").ap())
    build_rec(nc, *args)
    result = run_bass_kernel_spmd(nc, [arrays], core_ids=[0])
    return result.results[0]["out"]
```
